# Optimizing a Trainium2 kernel written in Bass

```python
import numpy as np
import jax
import jax.numpy as jnp

def _softmax(x, axis=-1):
    return jax.nn.softmax(x, axis=axis)

def _gelu(x):
    return jax.nn.gelu(x, approximate=True)

def _silu(x):
    return jax.nn.silu(x)

def _sigmoid(x):
    return jax.nn.sigmoid(x)

def _layernorm(x, axis=-1, eps=1e-05):
    m = jnp.mean(x, axis=axis, keepdims=True)
    v = jnp.var(x, axis=axis, keepdims=True)
    return (x - m) / jnp.sqrt(v + eps)

def _scatter_add(tgt, idx, src, axis=0):
    return tgt.at[idx].add(src)

def _segment_sum(src, seg, n):
    return jax.ops.segment_sum(src, seg, n)
kernel_name = 'mk_sandwich_d1_jaxref_r4_ad9cb4'

def setup_inputs(seed: int=0):
    np.random.seed(seed)
    _w = jnp.asarray

    def _L0_attn_setup():
        import jax, jax.numpy as jnp
        import numpy as np
        D_MODEL, N_HEADS = (256, 16)
        D_H = D_MODEL // N_HEADS
        D_HR = D_H // 2
        D_LATENT = 64
        THETA = 10000.0

        def rope(x, theta=THETA):
            S, d = (x.shape[-2], x.shape[-1])
            inv = theta ** (-jnp.arange(0, d, 2, dtype=jnp.float32) / d)
            ang = jnp.arange(S, dtype=jnp.float32)[:, None] * inv
            cos, sin = (jnp.cos(ang), jnp.sin(ang))
            x1, x2 = (x[..., 0::2], x[..., 1::2])
            r1 = x1 * cos - x2 * sin
            r2 = x1 * sin + x2 * cos
            return jnp.stack([r1, r2], axis=-1).reshape(x.shape)
        key = jax.random.key(seed)
        ks = jax.random.split(key, 9)
        s = lambda fan_in: 1.0 / np.sqrt(fan_in)
        return {'x': jax.random.normal(ks[0], (4, 512, D_MODEL), jnp.float32), 'W_DQ': jax.random.normal(ks[1], (D_MODEL, D_LATENT), jnp.float32) * s(D_MODEL), 'W_UQ': jax.random.normal(ks[2], (D_LATENT, N_HEADS * D_H), jnp.float32) * s(D_LATENT), 'W_QR': jax.random.normal(ks[3], (D_LATENT, N_HEADS * D_HR), jnp.float32) * s(D_LATENT), 'W_DKV': jax.random.normal(ks[4], (D_MODEL, D_LATENT), jnp.float32) * s(D_MODEL), 'W_UK': jax.random.normal(ks[5], (D_LATENT, N_HEADS * D_H), jnp.float32) * s(D_LATENT), 'W_UV': jax.random.normal(ks[6], (D_LATENT, N_HEADS * D_H), jnp.float32) * s(D_LATENT), 'W_KR': jax.random.normal(ks[7], (D_MODEL, D_HR), jnp.float32) * s(D_MODEL), 'W_O': jax.random.normal(ks[8], (N_HEADS * D_H, D_MODEL), jnp.float32) * s(N_HEADS * D_H)}
    _L0_attn_in = _L0_attn_setup()

    def _L0_ffn_setup():
        import jax, jax.numpy as jnp
        import numpy as np
        B, N, D = (4, 1024, 256)
        E, K, H, ITERS = (8, 2, 64, 2)
        DT = 0.1
        C = 2 * D

        def _gelu(x):
            return jax.nn.gelu(x, approximate=False)

        def _inl(ctrl, xs, vs, mu):
            a, b, g = jnp.split(ctrl, 3, axis=-1)
            v_next = jax.nn.sigmoid(a) * vs - jax.nn.softplus(b) * (xs - mu)
            x_next = xs + DT * jax.nn.sigmoid(g) * v_next
            return (x_next, v_next)

        def _experts(ctx, idx, w1, b1, w2, b2):
            out = jnp.zeros((ctx.shape[0], w2.shape[2]), ctx.dtype)
            for e in range(E):
                h = _gelu(ctx @ w1[e] + b1[e])
                o = h @ w2[e] + b2[e]
                out = out + jnp.where((idx == e)[:, None], o, jnp.float32(0))
            return out

        def _forward(x, integration_weight, mu, router_w1, router_b1, router_w2, router_b2, halt_w1, halt_b1, halt_w2, halt_b2, expert_w1, expert_b1, expert_w2, expert_b2, shared_w1, shared_b1, shared_w2, shared_b2, shared_weight, refine_w1, refine_b1, refine_w2, refine_b2):
            b, n, d = x.shape
            xf = x.reshape(b * n, d)
            logits = _gelu(xf @ router_w1 + router_b1) @ router_w2 + router_b2
            probs = jax.nn.softmax(logits, axis=-1)
            topk_p, topk_i = jax.lax.top_k(probs, K)
            topk_p = topk_p / jnp.sum(topk_p, axis=-1, keepdims=True)
            flat_idx = topk_i.reshape(-1)
            flat_w = topk_p.reshape(-1, 1)
            v = jnp.zeros_like(xf)
            integrated = xf
            for _ in range(ITERS):
                ctx = jnp.concatenate([integrated, v], axis=-1)
                shared_ctrl = _gelu(ctx @ shared_w1 + shared_b1) @ shared_w2 + shared_b2
                x_sh, v_sh = _inl(shared_ctrl, integrated, v, mu)
                sw = jax.nn.sigmoid(shared_weight)
                ctx_e = jnp.repeat(ctx, K, axis=0)
                x_e = jnp.repeat(integrated, K, axis=0)
                v_e = jnp.repeat(v, K, axis=0)
                ctrl = _experts(ctx_e, flat_idx, expert_w1, expert_b1, expert_w2, expert_b2)
                x_r, v_r = _inl(ctrl, x_e, v_e, mu)
                x_r = (x_r * flat_w).reshape(-1, K, d).sum(axis=1)
                v_r = (v_r * flat_w).reshape(-1, K, d).sum(axis=1)
                x_next = sw * x_sh + (1.0 - sw) * x_r
                v_next = sw * v_sh + (1.0 - sw) * v_r
                halt = jax.nn.sigmoid(_gelu(integrated @ halt_w1 + halt_b1) @ halt_w2 + halt_b2)
                integrated = integrated + halt * (x_next - integrated)
                v = v + halt * (v_next - v)
            refined = _gelu(integrated @ refine_w1 + refine_b1) @ refine_w2 + refine_b2
            out = xf + integration_weight * refined
            return out.reshape(b, n, d)
        key = jax.random.key(seed)
        ks = jax.random.split(key, 12)
        rn = lambda k, s, sc=0.02: jax.random.normal(k, s, dtype=jnp.float32) * sc
        z = lambda s: jnp.zeros(s, jnp.float32)
        return {'x': jax.random.normal(ks[0], (B, N, D), dtype=jnp.float32), 'integration_weight': jnp.full((D,), 0.5, jnp.float32), 'mu': z((D,)), 'router_w1': rn(ks[1], (D, D // 4)), 'router_b1': z((D // 4,)), 'router_w2': rn(ks[2], (D // 4, E)), 'router_b2': z((E,)), 'halt_w1': rn(ks[3], (D, D // 4)), 'halt_b1': z((D // 4,)), 'halt_w2': rn(ks[4], (D // 4, 1)), 'halt_b2': z((1,)), 'expert_w1': rn(ks[5], (E, C, H)), 'expert_b1': z((E, H)), 'expert_w2': rn(ks[6], (E, H, 3 * D)), 'expert_b2': z((E, 3 * D)), 'shared_w1': rn(ks[7], (C, H)), 'shared_b1': z((H,)), 'shared_w2': rn(ks[8], (H, 3 * D)), 'shared_b2': z((3 * D,)), 'shared_weight': jnp.float32(0.5), 'refine_w1': rn(ks[9], (D, 2 * D)), 'refine_b1': z((2 * D,)), 'refine_w2': rn(ks[10], (2 * D, D)), 'refine_b2': z((D,))}
    _L0_ffn_in = _L0_ffn_setup()
    _d = {'L0_attn_x': _L0_attn_in['x'], 'L0_attn_W_DQ': _L0_attn_in['W_DQ'], 'L0_attn_W_UQ': _L0_attn_in['W_UQ'], 'L0_attn_W_QR': _L0_attn_in['W_QR'], 'L0_attn_W_DKV': _L0_attn_in['W_DKV'], 'L0_attn_W_UK': _L0_attn_in['W_UK'], 'L0_attn_W_UV': _L0_attn_in['W_UV'], 'L0_attn_W_KR': _L0_attn_in['W_KR'], 'L0_attn_W_O': _L0_attn_in['W_O'], 'L0_ffn_integration_weight': _L0_ffn_in['integration_weight'], 'L0_ffn_mu': _L0_ffn_in['mu'], 'L0_ffn_router_w1': _L0_ffn_in['router_w1'], 'L0_ffn_router_b1': _L0_ffn_in['router_b1'], 'L0_ffn_router_w2': _L0_ffn_in['router_w2'], 'L0_ffn_router_b2': _L0_ffn_in['router_b2'], 'L0_ffn_halt_w1': _L0_ffn_in['halt_w1'], 'L0_ffn_halt_b1': _L0_ffn_in['halt_b1'], 'L0_ffn_halt_w2': _L0_ffn_in['halt_w2'], 'L0_ffn_halt_b2': _L0_ffn_in['halt_b2'], 'L0_ffn_expert_w1': _L0_ffn_in['expert_w1'], 'L0_ffn_expert_b1': _L0_ffn_in['expert_b1'], 'L0_ffn_expert_w2': _L0_ffn_in['expert_w2'], 'L0_ffn_expert_b2': _L0_ffn_in['expert_b2'], 'L0_ffn_shared_w1': _L0_ffn_in['shared_w1'], 'L0_ffn_shared_b1': _L0_ffn_in['shared_b1'], 'L0_ffn_shared_w2': _L0_ffn_in['shared_w2'], 'L0_ffn_shared_b2': _L0_ffn_in['shared_b2'], 'L0_ffn_shared_weight': _L0_ffn_in['shared_weight'], 'L0_ffn_refine_w1': _L0_ffn_in['refine_w1'], 'L0_ffn_refine_b1': _L0_ffn_in['refine_b1'], 'L0_ffn_refine_w2': _L0_ffn_in['refine_w2'], 'L0_ffn_refine_b2': _L0_ffn_in['refine_b2']}
    _x0 = _d['L0_attn_x']
    _d['L0_attn_x'] = jax.random.normal(jax.random.fold_in(jax.random.key(seed), 1), (8, 1024, 256), dtype=_x0.dtype)
    del _x0
    return _d

def reference(L0_attn_x, L0_attn_W_DQ, L0_attn_W_UQ, L0_attn_W_QR, L0_attn_W_DKV, L0_attn_W_UK, L0_attn_W_UV, L0_attn_W_KR, L0_attn_W_O, L0_ffn_integration_weight, L0_ffn_mu, L0_ffn_router_w1, L0_ffn_router_b1, L0_ffn_router_w2, L0_ffn_router_b2, L0_ffn_halt_w1, L0_ffn_halt_b1, L0_ffn_halt_w2, L0_ffn_halt_b2, L0_ffn_expert_w1, L0_ffn_expert_b1, L0_ffn_expert_w2, L0_ffn_expert_b2, L0_ffn_shared_w1, L0_ffn_shared_b1, L0_ffn_shared_w2, L0_ffn_shared_b2, L0_ffn_shared_weight, L0_ffn_refine_w1, L0_ffn_refine_b1, L0_ffn_refine_w2, L0_ffn_refine_b2):

    def _L0_attn_ref(x, W_DQ, W_UQ, W_QR, W_DKV, W_UK, W_UV, W_KR, W_O):
        import jax, jax.numpy as jnp
        import numpy as np
        D_MODEL, N_HEADS = (256, 16)
        D_H = D_MODEL // N_HEADS
        D_HR = D_H // 2
        D_LATENT = 64
        THETA = 10000.0

        def rope(x, theta=THETA):
            S, d = (x.shape[-2], x.shape[-1])
            inv = theta ** (-jnp.arange(0, d, 2, dtype=jnp.float32) / d)
            ang = jnp.arange(S, dtype=jnp.float32)[:, None] * inv
            cos, sin = (jnp.cos(ang), jnp.sin(ang))
            x1, x2 = (x[..., 0::2], x[..., 1::2])
            r1 = x1 * cos - x2 * sin
            r2 = x1 * sin + x2 * cos
            return jnp.stack([r1, r2], axis=-1).reshape(x.shape)
        B, S, _ = x.shape
        d_qk = D_H + D_HR
        c_q = x @ W_DQ
        Qc = (c_q @ W_UQ).reshape(B, S, N_HEADS, D_H).transpose(0, 2, 1, 3)
        Qr = (c_q @ W_QR).reshape(B, S, N_HEADS, D_HR).transpose(0, 2, 1, 3)
        Qr = rope(Qr)
        c_kv = x @ W_DKV
        Kc = (c_kv @ W_UK).reshape(B, S, N_HEADS, D_H).transpose(0, 2, 1, 3)
        Kr = rope((x @ W_KR)[:, None, :, :])
        Kr = jnp.broadcast_to(Kr, (B, N_HEADS, S, D_HR))
        V = (c_kv @ W_UV).reshape(B, S, N_HEADS, D_H).transpose(0, 2, 1, 3)
        Q = jnp.concatenate([Qc, Qr], axis=-1)
        K = jnp.concatenate([Kc, Kr], axis=-1)
        scores = jnp.einsum('bhqd,bhkd->bhqk', Q, K)
        scores = jnp.clip(scores, -80.0, 80.0)
        causal = jnp.tril(jnp.ones((S, S), dtype=bool))
        scores = jnp.where(causal, scores, -jnp.inf)
        weights = jax.nn.softmax(scores / jnp.sqrt(jnp.float32(d_qk)), axis=-1)
        attn = jnp.einsum('bhqk,bhkd->bhqd', weights, V)
        attn = attn.transpose(0, 2, 1, 3).reshape(B, S, N_HEADS * D_H)
        return attn @ W_O

    def _L0_ffn_ref(x, integration_weight, mu, router_w1, router_b1, router_w2, router_b2, halt_w1, halt_b1, halt_w2, halt_b2, expert_w1, expert_b1, expert_w2, expert_b2, shared_w1, shared_b1, shared_w2, shared_b2, shared_weight, refine_w1, refine_b1, refine_w2, refine_b2):
        import jax, jax.numpy as jnp
        import numpy as np
        B, N, D = (4, 1024, 256)
        E, K, H, ITERS = (8, 2, 64, 2)
        DT = 0.1
        C = 2 * D

        def _gelu(x):
            return jax.nn.gelu(x, approximate=False)

        def _inl(ctrl, xs, vs, mu):
            a, b, g = jnp.split(ctrl, 3, axis=-1)
            v_next = jax.nn.sigmoid(a) * vs - jax.nn.softplus(b) * (xs - mu)
            x_next = xs + DT * jax.nn.sigmoid(g) * v_next
            return (x_next, v_next)

        def _experts(ctx, idx, w1, b1, w2, b2):
            out = jnp.zeros((ctx.shape[0], w2.shape[2]), ctx.dtype)
            for e in range(E):
                h = _gelu(ctx @ w1[e] + b1[e])
                o = h @ w2[e] + b2[e]
                out = out + jnp.where((idx == e)[:, None], o, jnp.float32(0))
            return out

        def _forward(x, integration_weight, mu, router_w1, router_b1, router_w2, router_b2, halt_w1, halt_b1, halt_w2, halt_b2, expert_w1, expert_b1, expert_w2, expert_b2, shared_w1, shared_b1, shared_w2, shared_b2, shared_weight, refine_w1, refine_b1, refine_w2, refine_b2):
            b, n, d = x.shape
            xf = x.reshape(b * n, d)
            logits = _gelu(xf @ router_w1 + router_b1) @ router_w2 + router_b2
            probs = jax.nn.softmax(logits, axis=-1)
            topk_p, topk_i = jax.lax.top_k(probs, K)
            topk_p = topk_p / jnp.sum(topk_p, axis=-1, keepdims=True)
            flat_idx = topk_i.reshape(-1)
            flat_w = topk_p.reshape(-1, 1)
            v = jnp.zeros_like(xf)
            integrated = xf
            for _ in range(ITERS):
                ctx = jnp.concatenate([integrated, v], axis=-1)
                shared_ctrl = _gelu(ctx @ shared_w1 + shared_b1) @ shared_w2 + shared_b2
                x_sh, v_sh = _inl(shared_ctrl, integrated, v, mu)
                sw = jax.nn.sigmoid(shared_weight)
                ctx_e = jnp.repeat(ctx, K, axis=0)
                x_e = jnp.repeat(integrated, K, axis=0)
                v_e = jnp.repeat(v, K, axis=0)
                ctrl = _experts(ctx_e, flat_idx, expert_w1, expert_b1, expert_w2, expert_b2)
                x_r, v_r = _inl(ctrl, x_e, v_e, mu)
                x_r = (x_r * flat_w).reshape(-1, K, d).sum(axis=1)
                v_r = (v_r * flat_w).reshape(-1, K, d).sum(axis=1)
                x_next = sw * x_sh + (1.0 - sw) * x_r
                v_next = sw * v_sh + (1.0 - sw) * v_r
                halt = jax.nn.sigmoid(_gelu(integrated @ halt_w1 + halt_b1) @ halt_w2 + halt_b2)
                integrated = integrated + halt * (x_next - integrated)
                v = v + halt * (v_next - v)
            refined = _gelu(integrated @ refine_w1 + refine_b1) @ refine_w2 + refine_b2
            out = xf + integration_weight * refined
            return out.reshape(b, n, d)
        return _forward(x, integration_weight, mu, router_w1, router_b1, router_w2, router_b2, halt_w1, halt_b1, halt_w2, halt_b2, expert_w1, expert_b1, expert_w2, expert_b2, shared_w1, shared_b1, shared_w2, shared_b2, shared_weight, refine_w1, refine_b1, refine_w2, refine_b2)
    x = L0_attn_x
    x = x + _layernorm(_L0_attn_ref(_layernorm(x, axis=-1), L0_attn_W_DQ, L0_attn_W_UQ, L0_attn_W_QR, L0_attn_W_DKV, L0_attn_W_UK, L0_attn_W_UV, L0_attn_W_KR, L0_attn_W_O), axis=-1)
    x = x + _layernorm(_L0_ffn_ref(_layernorm(x, axis=-1), L0_ffn_integration_weight, L0_ffn_mu, L0_ffn_router_w1, L0_ffn_router_b1, L0_ffn_router_w2, L0_ffn_router_b2, L0_ffn_halt_w1, L0_ffn_halt_b1, L0_ffn_halt_w2, L0_ffn_halt_b2, L0_ffn_expert_w1, L0_ffn_expert_b1, L0_ffn_expert_w2, L0_ffn_expert_b2, L0_ffn_shared_w1, L0_ffn_shared_b1, L0_ffn_shared_w2, L0_ffn_shared_b2, L0_ffn_shared_weight, L0_ffn_refine_w1, L0_ffn_refine_b1, L0_ffn_refine_w2, L0_ffn_refine_b2), axis=-1)
    return x

_drawn_inputs = setup_inputs


def setup_inputs(seed=0):
    import zlib

    import numpy as np

    out = dict(_drawn_inputs(seed))
    spreads = {'L0_ffn_integration_weight': (0.5, 0.6),
     'L0_ffn_mu': (0.0, 2.0),
     'L0_ffn_router_b1': (0.0, 2.0),
     'L0_ffn_router_b2': (0.0, 2.0),
     'L0_ffn_halt_b1': (0.0, 2.0),
     'L0_ffn_expert_b1': (0.0, 2.0),
     'L0_ffn_expert_b2': (0.0, 2.0),
     'L0_ffn_shared_b1': (0.0, 2.0),
     'L0_ffn_shared_b2': (0.0, 2.0),
     'L0_ffn_refine_b1': (0.0, 0.8),
     'L0_ffn_refine_b2': (0.0, 0.377)}
    factors = {'L0_ffn_router_w1': 51.346,
     'L0_ffn_router_w2': 37.448,
     'L0_ffn_halt_w1': 8.0,
     'L0_ffn_halt_w2': 8.0,
     'L0_ffn_expert_w1': 43.178,
     'L0_ffn_expert_w2': 36.894,
     'L0_ffn_shared_w1': 25.025,
     'L0_ffn_shared_w2': 8.0,
     'L0_ffn_refine_w1': 3.594,
     'L0_ffn_refine_w2': 3.34}
    for name, (base, spread) in spreads.items():
        noise = np.random.default_rng([zlib.crc32(name.encode()), seed]).standard_normal(out[name].shape)
        drawn = base * np.exp(spread * noise) if base else spread * noise
        out[name] = jnp.asarray(drawn.astype(out[name].dtype))
    for name, factor in factors.items():
        out[name] = (out[name] * factor).astype(out[name].dtype)
    return out
```

```python
from contextlib import ExitStack

import numpy as np

import concourse.bass as bass
from concourse import mybir

F32 = mybir.dt.float32
F32R = mybir.dt.float32r
F16 = mybir.dt.float16
BF16 = mybir.dt.bfloat16
U32 = mybir.dt.uint32
ALU = mybir.AluOpType
ACT = mybir.ActivationFunctionType

P = 128
BATCH, SEQ, D = 8, 1024, 256
TOKENS = BATCH * SEQ
TILES = SEQ // P
HEADS, HEAD, ROPE_DIM = 16, 16, 8
GROUPS = HEADS // 4
CHUNKS = SEQ // 512
CLIP = 80.0
EPS = 1e-5
PROB_SETS = 6
QK_UP = 16.0
PV_LAG = 2
DVE_STEPS_A = 3 + 4 + 8 + 3

BLOCK = 512
BT = BLOCK // P
EXPERTS, HIDDEN = 8, 64
MC = EXPERTS * HIDDEN // P
HALF_STEP = 0.05
DVE_STEPS_F = 131


def attention(nc, x_dram, consts_dram, w_dram, x1_dram):
    dh, dr, heads = HEAD, ROPE_DIM, HEADS
    x_v = x_dram.rearrange("(b t p) d -> b p t d", p=P, t=TILES)
    x1_v = x1_dram.rearrange("(b t p) d -> b p t d", p=P, t=TILES)
    qk_scale = 1.0 / np.sqrt(float(dh + dr))
    exp_hi = float(np.exp(CLIP * qk_scale))
    exp_lo = float(np.exp(-CLIP * qk_scale))
    exp_scale = float(qk_scale / QK_UP ** 2)

    XT, LATENT, HALF, V_ROWS, OUT_T, OUT_ROWS = 0, 4, 6, 20, 24, 28
    K_ROPE, Q_ROPE, K_HEADS, Q_HEADS, HALF_JOBS = 0, 1, 3, 5, 7
    JOBS = 32
    bank_of = [n % 8 for n in range(OUT_T)] + [0, 1, 2, 3, 4, 5, 6, 7]
    act_order = list(range(XT, HALF))
    for half in range(2):
        first = HALF + HALF_JOBS * half + K_HEADS
        act_order += [first, first + 1, f"q_rope{half}", first + 2, first + 3]
    act_order += list(range(OUT_T, OUT_ROWS))
    BLOCKS = 3
    K_ORDER, Q_ORDER = (0, 0, 1), (0, 1, 0)

    steps = [(c, g, j) for c in range(CHUNKS) for g in range(GROUPS) for j in range(4 * c + 4)]
    STEPS = len(steps)
    last_step = {}
    for s, (c, g, j) in enumerate(steps):
        last_step[c * GROUPS + g] = s
    ACCS = CHUNKS * GROUPS

    with ExitStack() as ctx:
        def sb(name, shape, dt=F32):
            return ctx.enter_context(nc.sbuf_tensor(name, shape, dt))

        def sem(name):
            return ctx.enter_context(nc.semaphore(name))

        psum = ctx.enter_context(nc.psum_tensor("psum_a", [P, 8, 512], F32))
        ident = sb("ident_a", [P, P])
        w_latent = sb("w_latent", [P, 2, 2, 128], F32R)
        w_kr = sb("w_kr", [P, 2, 2, 128], F32R)
        w_qr = sb("w_qr", [64, 2, 2, heads * dr], F32R)
        w_q = sb("w_q", [64, 2, D], F32R)
        w_kv = sb("w_kv", [P, 2, 2, D], F32R)
        w_o = sb("w_o", [P, 2, 2, D], F32R)
        cos = sb("cos", [P, SEQ])
        sin = sb("sin", [P, SEQ])
        tri = sb("tri", [P, 2, P])
        x_in = sb("x_in", [P, TILES, D])
        xn = sb("xn", [P, TILES, D])
        y = xn
        xn_t = sb("xn_t", [P, 2, 2, SEQ], F32R)
        attn_t = xn_t
        latent_t = sb("latent_t", [P, 2, SEQ], F32R)
        rope = sb("rope", [P, 2, 2, 512])
        rope_a, rope_b = rope[:, 0], rope[:, 1]
        x_res = rope[:].rearrange("p a h (t d) -> p (a h t) d", d=D)
        k_stack = sb("k_stack", [BLOCKS * (dh + dr), heads, SEQ], F16)
        q_stack = sb("q_stack", [BLOCKS * (dh + dr), heads, SEQ], F16)
        heads_dram = nc.dram_tensor("heads_scratch", (2, 2, 2 * P, SEQ), F16, kind="Internal").ap()
        rope_dram = nc.dram_tensor("rope_scratch", (2, P, SEQ), F16, kind="Internal").ap()
        v = sb("v", [P, TILES, heads, 32])
        probs = sb("probs", [P, PROB_SETS, 2, 512])
        late_parts = sb("late_parts", [P, 6 * SEQ], F16)
        halves = (probs[:].rearrange("p s u n -> p (s u n)").bitcast(F16)[:, 0:6 * SEQ], late_parts[:])
        kq_parts = [p[:, 0:4 * SEQ].rearrange("p (f a m n) -> p f a m n", f=2, a=2, m=2) for p in halves]
        q_rope_parts = [p[:, 4 * SEQ:5 * SEQ].rearrange("p (a n) -> p a n", a=2) for p in halves]
        k_rope_parts = [p[0:dr, 5 * SEQ:6 * SEQ].rearrange("p (a n) -> p a n", a=2) for p in halves]
        raw = probs[:].rearrange("p s u n -> p (s u n)")
        raw_kv = raw[:, 0:512].rearrange("p (f n) -> p f n", f=2)
        raw_kr = raw[:, 512:768].rearrange("p (k n) -> p k n", k=2)
        raw_latent = raw[:, 768:1024].rearrange("p (k n) -> p k n", k=2)
        raw_qr = raw[0:64, 1024:1280].rearrange("p (f h r) -> p f h r", f=2, r=dr)
        raw_q = raw[0:64, 1280:1536]
        raw_o = raw[:, 1536:2048].rearrange("p (k n) -> p k n", k=2)
        acc_sb = sb("acc_sb", [P, 2, 512])
        recip = sb("recip", [P, 2, 4, 4])
        attn = sb("attn", [P, TILES, D])
        q_rope = sb("q_rope", [P, SEQ])
        k_rope = attn[0:dr, 4:8, :].rearrange("p t d -> p (t d)")
        stats = sb("stats", [P, TILES, 6])
        moments = sb("moments", [P, 3, TILES])
        mean = sb("mean", [P, 2, TILES])
        veps = sb("veps", [P, 2, TILES])
        rstd = sb("rstd", [P, 2, TILES])
        half_neg = sb("half_neg", [P, TILES])

        weights_in = sem("weights_in")
        cleared = sem("cleared")
        weights_ready = sem("weights_ready")
        x_loaded = sem("x_loaded")
        xres_loaded = sem("xres_loaded")
        stats_ready = sem("stats_ready")
        rstd_ready = sem("rstd_ready")
        xn_ready = sem("xn_ready")
        job_done = sem("job_done")
        act_evac = sem("act_evac")
        dve_evac = sem("dve_evac")
        dve_step = sem("dve_step")
        k_rope_done = sem("k_rope_done")
        q_rope_sum = sem("q_rope_sum")
        q_rope_done = sem("q_rope_done")
        heads_done = sem("heads_done")
        scratch_written = [sem(f"scratch_written{half}") for half in range(2)]
        stacked = [sem(f"stacked{half}") for half in range(2)]
        scores_ready = sem("scores_ready")
        exp_done = sem("exp_done")
        clip_done = sem("clip_done")
        pv_done = sem("pv_done")
        acc_copied = sem("acc_copied")
        acc_turned = sem("acc_turned")
        attn_ready = sem("attn_ready")
        y_ready = sem("y_ready")
        pool_dma_done = sem("pool_dma_done")


        def act_value(b, job):
            return b * len(act_order) + act_order.index(job) + 1

        def bank_read(eng, b, job):
            eng.wait_ge(dve_evac, b * JOBS + job + 1)

        block = ctx.enter_context(nc.Block())
        N_WEIGHTS = 10

        @block.sync
        def _(sp):
            for dst, src in ((cos[:], consts_dram["cos"]), (sin[:], consts_dram["sin"]),
                             (raw_latent[:, :, 0:64], w_dram["W_DQ"].rearrange("(k p) n -> p k n", p=P)),
                             (raw_latent[:, :, 64:128], w_dram["W_DKV"].rearrange("(k p) n -> p k n", p=P)),
                             (raw_qr[:, 0], w_dram["W_QR"].rearrange("p (h r) -> p h r", r=dr)),
                             (raw_q, w_dram["W_UQ"]),
                             (raw_kv[64:128, 0], w_dram["W_UK"]), (raw_kv[64:128, 1], w_dram["W_UV"]),
                             (raw_o, w_dram["W_O"].rearrange("(k p) n -> p k n", p=P))):
                sp.dma_start(dst, src).then_inc(weights_in, 16)
            sp.wait_ge(cleared, 1)
            sp.dma_start(raw_kr[:, :, 0:dr], w_dram["W_KR"].rearrange("(k p) n -> p k n", p=P)).then_inc(weights_in, 16)
            with sp.Fori(0, BATCH) as b:
                sp.dma_start(x_in[:], x_v[b]).then_inc(x_loaded, 16)

                for half in range(2):
                    cols = slice(512 * half, 512 * half + 512)
                    sp.wait_ge(k_rope_done, 2 * b + half + 1)
                    for i, part in enumerate(K_ORDER):
                        row = i * (dh + dr) + dh
                        sp.dma_start(k_stack[row:row + dr, :, cols],
                                     k_rope_parts[half][:, part, :].unsqueeze(1).to_broadcast([dr, heads, 512])).then_inc(stacked[half], 16)
                    sp.wait_ge(q_rope_done, 2 * b + half + 1)
                    sp.dma_start(rope_dram[:, :, cols].rearrange("a p n -> p a n"), q_rope_parts[half][:, :, :]).then_inc(scratch_written[half], 16)
                    sp.wait_ge(heads_done, 2 * b + half + 1)
                    for f in range(2):
                        for part in range(2):
                            sp.dma_start(heads_dram[f, part, :, cols].rearrange("(m p) n -> p m n", p=P),
                                         kq_parts[half][:, f, part, :, :]).then_inc(scratch_written[half], 16)
                    sp.wait_ge(scratch_written[half], (b + 1) * 16 * 5)
                    for f, (dst, order) in enumerate(((k_stack, K_ORDER), (q_stack, Q_ORDER))):
                        for i, part in enumerate(order):
                            row = i * (dh + dr)
                            sp.dma_start(dst[row:row + dh, :, cols],
                                         heads_dram[f, part, :, cols].rearrange("(h r) n -> r h n", r=dh)).then_inc(stacked[half], 16)
                    for i, part in enumerate(Q_ORDER):
                        row = i * (dh + dr) + dh
                        sp.dma_start(q_stack[row:row + dr, :, cols],
                                     rope_dram[part, :, cols].rearrange("(h r) n -> r h n", r=dr)).then_inc(stacked[half], 16)
                sp.dma_start(x_res, x_v[b]).then_inc(xres_loaded, 16)

        @block.gpsimd
        def _(pool):
            pool.dma_start(ident[:], consts_dram["ident"]).then_inc(pool_dma_done, 16)
            pool.memset(raw_kr, 0.0)
            pool.memset(v[:], 0.0)
            pool.memset(tri[:], exp_hi)
            pool.memset(half_neg[:], -0.5).then_inc(cleared, 1)
            pool.wait_ge(cleared, 1)
            pool.memset(v[:, :, :, dh:dh + 1], 1.0)
            pool.affine_select(out=tri[:], in_=tri[:], compare_op=ALU.is_ge, fill=0.0, base=0,
                               pattern=[[0, 2], [1, P]], channel_multiplier=-1).then_inc(cleared, 1)

            with pool.Fori(0, BATCH) as b:
                pool.wait_ge(stats_ready, 2 * b + 1)
                pool.tensor_tensor(rstd[:, 0], veps[:, 0], half_neg[:], ALU.pow).then_inc(rstd_ready, 1)
                for half in range(2):
                    cols = slice(512 * half, 512 * half + 512)
                    bank_read(pool, b, HALF + HALF_JOBS * half + Q_ROPE + 1)
                    pool.tensor_tensor(q_rope[:, cols], rope_a[:, half], rope_b[:, half], ALU.add).then_inc(q_rope_sum, 1)
                    pool.wait_ge(act_evac, act_value(b, f"q_rope{half}"))
                    pool.tensor_tensor(q_rope_parts[half][:, 1, :], q_rope[:, cols], q_rope_parts[half][:, 0, :],
                                       ALU.subtract).then_inc(q_rope_done, 1)
                pool.wait_ge(stats_ready, 2 * b + 2)
                pool.tensor_tensor(rstd[:, 1], veps[:, 1], half_neg[:], ALU.pow).then_inc(rstd_ready, 1)
                pool.wait_ge(y_ready, b + 1)
                pool.dma_start(x1_v[b], y[:]).then_inc(pool_dma_done, 16)
            pool.wait_ge(pool_dma_done, 16 * (BATCH + 1))

        @block.scalar
        def _(act):
            with act.Fori(0, BATCH) as b:
                def upper(job, dst):
                    act.wait_ge(job_done, b * JOBS + job + 1)
                    act.activation(dst, psum[:, bank_of[job], :], ACT.Copy).then_inc(act_evac, 1)

                for n in range(4):
                    upper(XT + n, xn_t[:, 0, n % 2, 512 * (n // 2):512 * (n // 2) + 512])
                for half in range(2):
                    upper(LATENT + half, latent_t[:, 0, 512 * half:512 * half + 512])
                for half in range(2):
                    cols = slice(512 * half, 512 * half + 512)
                    for n in range(4):
                        upper(HALF + HALF_JOBS * half + K_HEADS + n, kq_parts[half][:, n // 2, 0, n % 2, :])
                        if n == 1:
                            act.wait_ge(q_rope_sum, 2 * b + half + 1)
                            act.activation(q_rope_parts[half][:, 0, :], q_rope[:, cols], ACT.Copy).then_inc(act_evac, 1)
                for s, (c, g, j) in enumerate(steps):
                    q0 = 128 * max(0, j - 4 * c)
                    for u in range(2):
                        n = 2 * s + u
                        act.wait_ge(scores_ready, b * 2 * STEPS + n + 1)
                        if n >= PROB_SETS:
                            act.wait_ge(pv_done, b * STEPS + (n - PROB_SETS) // 2 + 1)
                        bank = 2 * (n % 3)
                        act.activation(probs[:, n % PROB_SETS, :, q0:512], psum[:, bank:bank + 2, q0:512], ACT.Exp,
                                       scale=exp_scale).then_inc(exp_done, 1)
                for n in range(4):
                    upper(OUT_T + n, attn_t[:, 0, n % 2, 512 * (n // 2):512 * (n // 2) + 512])

        @block.vector
        def _(dve):
            dve.wait_ge(weights_in, 16 * N_WEIGHTS)
            for i in range(2):
                dve.tensor_copy(raw_qr[:, 1, :, i:dr:2], raw_qr[:, 0, :, 1 - i:dr:2])
                last = dve.tensor_copy(raw_kr[:, :, 32 + i:32 + dr:2], raw_kr[:, :, 1 - i:dr:2])
            last.then_inc(weights_ready, 1)
            dve.wait_ge(weights_ready, 1)
            shares = ((w_latent[:, 0], w_latent[:, 1], raw_latent, 1.0), (w_kr[:, 0], w_kr[:, 1], raw_kr, 1.0),
                      (w_qr[:, 0], w_qr[:, 1], raw_qr.rearrange("p f h r -> p f (h r)"), 1.0),
                      (w_q[:, 0], w_q[:, 1], raw_q, QK_UP),
                      (w_kv[64:128, 0, 0], w_kv[64:128, 1, 0], raw_kv[64:128, 0], QK_UP),
                      (w_kv[64:128, 0, 1], w_kv[64:128, 1, 1], raw_kv[64:128, 1], 1.0),
                      (w_o[:, 0], w_o[:, 1], raw_o, 1.0))
            for hi, _, src, scale in shares:
                last = dve.tensor_scalar(hi, src, scale, None, ALU.mult)
            last.then_inc(weights_ready, 1)
            dve.wait_ge(weights_ready, 2)
            for hi, lo, src, scale in shares:
                last = dve.scalar_tensor_tensor(out=lo, in0=src, scalar=scale, in1=hi.bitcast(F32),
                                                op0=ALU.mult, op1=ALU.subtract)
            last.then_inc(weights_ready, 1)
            with dve.Fori(0, BATCH) as b:
                made = [0]

                def then_wait(ins):
                    made[0] += 1
                    ins.then_inc(dve_step, 1)
                    dve.wait_ge(dve_step, b * DVE_STEPS_A + made[0])

                def layernorm_moments(which):
                    dve.tensor_tensor(moments[:, 0], stats[:, :, 1], stats[:, :, 4], ALU.add)
                    dve.tensor_tensor(moments[:, 1], stats[:, :, 1], stats[:, :, 4], ALU.subtract)
                    then_wait(dve.tensor_tensor(moments[:, 2], stats[:, :, 2], stats[:, :, 5], ALU.add))
                    dve.tensor_scalar(mean[:, which], moments[:, 0], 0.5, None, ALU.mult)
                    dve.tensor_scalar(moments[:, 2], moments[:, 2], 1.0 / D, EPS, ALU.mult, ALU.add)
                    then_wait(dve.tensor_tensor(moments[:, 1], moments[:, 1], moments[:, 1], ALU.mult))
                    dve.scalar_tensor_tensor(out=veps[:, which], in0=moments[:, 1], scalar=0.25, in1=moments[:, 2],
                                             op0=ALU.mult, op1=ALU.add).then_inc(stats_ready, 1)

                dve.wait_ge(x_loaded, b * 16 + 16)
                for t in range(TILES):
                    last = dve.bn_stats(stats[:, t, :], x_in[:, t, :])
                then_wait(last)
                layernorm_moments(0)
                dve.wait_ge(rstd_ready, 2 * b + 1)
                dve.wait_ge(pool_dma_done, 16 * b + 16)
                for t in range(TILES):
                    last = dve.tensor_scalar(xn[:, t, :], x_in[:, t, :], mean[:, 0, t:t + 1], rstd[:, 0, t:t + 1],
                                             ALU.subtract, ALU.mult)
                last.then_inc(xn_ready, 1)

                def lower(job, hi, lo):
                    dve.wait_ge(act_evac, act_value(b, job))
                    return dve.tensor_tensor(lo, psum[:, bank_of[job], :], hi, ALU.subtract).then_inc(dve_evac, 1)

                for n in range(4):
                    at = (n % 2, slice(512 * (n // 2), 512 * (n // 2) + 512))
                    lower(XT + n, xn_t[:, 0, at[0], at[1]].bitcast(F32), xn_t[:, 1, at[0], at[1]])
                for half in range(2):
                    cols = slice(512 * half, 512 * half + 512)
                    lower(LATENT + half, latent_t[:, 0, cols].bitcast(F32), latent_t[:, 1, cols])
                for half in range(2):
                    cols = slice(512 * half, 512 * half + 512)
                    first = HALF + HALF_JOBS * half
                    bank = bank_of[first + K_ROPE]
                    dve.wait_ge(job_done, b * JOBS + first + K_ROPE + 1)
                    dve.tensor_tensor(k_rope[:, cols], psum[0:dr, bank, :], cos[0:dr, cols], ALU.mult)
                    dve.tensor_tensor(rope_a[0:dr, half], psum[32:32 + dr, bank, :], sin[32:32 + dr, cols],
                                      ALU.mult).then_inc(dve_evac, 1)
                    bank_read(dve, b, first + K_ROPE)
                    then_wait(dve.tensor_tensor(k_rope[:, cols], k_rope[:, cols], rope_a[0:dr, half], ALU.add))
                    then_wait(dve.tensor_copy(k_rope_parts[half][:, 0, :], k_rope[:, cols]))
                    dve.tensor_tensor(k_rope_parts[half][:, 1, :], k_rope[:, cols], k_rope_parts[half][:, 0, :],
                                      ALU.subtract).then_inc(k_rope_done, 1)
                    for dst, table, n in ((rope_a, cos, Q_ROPE), (rope_b, sin, Q_ROPE + 1)):
                        dve.wait_ge(job_done, b * JOBS + first + n + 1)
                        dve.tensor_tensor(dst[:, half], psum[:, bank_of[first + n], :], table[:, cols], ALU.mult).then_inc(dve_evac, 1)
                    for n in range(4):
                        lower(first + K_HEADS + n, kq_parts[half][:, n // 2, 0, n % 2, :], kq_parts[half][:, n // 2, 1, n % 2, :])
                    bank_read(dve, b, first + K_HEADS + 3)
                    dve.sem_inc(heads_done, 1)
                for n in range(4):
                    dve.wait_ge(job_done, b * JOBS + V_ROWS + n + 1)
                    dve.tensor_copy(v[:, 2 * n:2 * n + 2, :, 0:dh],
                                    psum[:, bank_of[V_ROWS + n], :].rearrange("p (t h d) -> p t h d", t=2, d=dh)).then_inc(dve_evac, 1)

                def copy_acc(ci):
                    dve.wait_ge(pv_done, b * STEPS + last_step[ci] + 1)
                    dve.tensor_copy(acc_sb[:, ci % 2, :], psum[:, 6 + ci % 2, :]).then_inc(acc_copied, 1)

                def divide(ci):
                    c, g = divmod(ci, GROUPS)
                    dve.wait_ge(acc_turned, b * ACCS + ci + 1)
                    turned = psum[:, 6 + ci % 2, :].rearrange("p (t u d) -> p t u d", t=4, u=4)
                    then_wait(dve.reciprocal(recip[:, ci % 2], turned[:, :, :, dh]))
                    dst = attn[:, 4 * c:4 * c + 4, 4 * g * dh:4 * (g + 1) * dh].rearrange("p t (u d) -> p t u d", d=dh)
                    dve.tensor_tensor(dst, turned[:, :, :, 0:dh],
                                      recip[:, ci % 2].unsqueeze(3).to_broadcast([P, 4, 4, dh]),
                                      ALU.mult).then_inc(attn_ready, 1)

                for s, (c, g, j) in enumerate(steps):
                    diag = j >= 4 * c
                    q0 = 128 * (j - 4 * c) if diag else 0
                    for u in range(2):
                        n = 2 * s + u
                        dve.wait_ge(exp_done, b * 2 * STEPS + n + 1)
                        pr = probs[:, n % PROB_SETS]
                        if diag:
                            last = dve.scalar_tensor_tensor(out=pr[:, :, q0:q0 + 128], in0=pr[:, :, q0:q0 + 128],
                                                            scalar=exp_lo, in1=tri[:], op0=ALU.max, op1=ALU.min)
                        w0 = q0 + 128 if diag else 0
                        if w0 < 512:
                            last = dve.tensor_scalar(pr[:, :, w0:512], pr[:, :, w0:512], exp_lo, exp_hi, ALU.max, ALU.min)
                        last.then_inc(clip_done, 1)
                    for ci in range(ACCS):
                        if s == last_step[ci] + PV_LAG + 1:
                            copy_acc(ci)
                        if s == last_step[ci] + PV_LAG + 3:
                            divide(ci)
                for ci in range(ACCS):
                    if last_step[ci] + PV_LAG + 1 >= STEPS:
                        copy_acc(ci)
                    if last_step[ci] + PV_LAG + 3 >= STEPS:
                        divide(ci)
                for n in range(4):
                    at = (n % 2, slice(512 * (n // 2), 512 * (n // 2) + 512))
                    lower(OUT_T + n, attn_t[:, 0, at[0], at[1]].bitcast(F32), attn_t[:, 1, at[0], at[1]])
                for t in range(TILES):
                    if t % 2 == 0:
                        dve.wait_ge(job_done, b * JOBS + OUT_ROWS + t // 2 + 1)
                    row = psum[:, bank_of[OUT_ROWS + t // 2], 256 * (t % 2):256 * (t % 2) + 256]
                    last = dve.bn_stats(stats[:, t, :], row)
                then_wait(last)
                layernorm_moments(1)
                dve.wait_ge(rstd_ready, 2 * b + 2)
                for t in range(TILES):
                    row = psum[:, bank_of[OUT_ROWS + t // 2], 256 * (t % 2):256 * (t % 2) + 256]
                    last = dve.tensor_scalar(y[:, t, :], row, mean[:, 1, t:t + 1], rstd[:, 1, t:t + 1],
                                             ALU.subtract, ALU.mult)
                    if t % 2:
                        last.then_inc(dve_evac, 1)
                bank_read(dve, b, JOBS - 1)
                dve.wait_ge(xres_loaded, b * 16 + 16)
                dve.tensor_tensor(y[:], y[:], x_res, ALU.add).then_inc(y_ready, 1)
                assert made[0] == DVE_STEPS_A, made[0]

        @block.tensor
        def _(pe):
            pe.wait_ge(pool_dma_done, 16)
            pe.wait_ge(weights_ready, 3)
            pe.wait_ge(cleared, 2)

            def product(out, w_hi, w_lo, x_hi, x_lo, start, stop):
                pe.matmul(out, w_hi, x_hi, start=start, stop=False)
                pe.matmul(out, w_lo, x_hi, start=False, stop=False)
                return pe.matmul(out, w_hi, x_lo, start=False, stop=stop)

            with pe.Fori(0, BATCH) as b:
                def bank_free(job):
                    if 8 <= job < OUT_T:
                        bank_read(pe, b, job - 8)

                pe.wait_ge(xn_ready, b + 1)
                for n in range(4):
                    half, k = divmod(n, 2)
                    for t in range(4):
                        last = pe.transpose(psum[:, bank_of[XT + n], 128 * t:128 * t + 128],
                                            xn[:, 4 * half + t, 128 * k:128 * k + 128], ident[:])
                    last.then_inc(job_done, 1)
                def from_x(job, w, half):
                    cols = slice(512 * half, 512 * half + 512)
                    for k in range(2):
                        bank_read(pe, b, XT + 2 * half + k)
                        last = product(psum[:, bank_of[job], :], w[:, 0, k, :], w[:, 1, k, :],
                                       xn_t[:, 0, k, cols], xn_t[:, 1, k, cols], k == 0, k == 1)
                    last.then_inc(job_done, 1)

                for half in range(2):
                    from_x(LATENT + half, w_latent, half)
                for half in range(2):
                    cols = slice(512 * half, 512 * half + 512)
                    first = HALF + HALF_JOBS * half
                    bank_free(first + K_ROPE)
                    from_x(first + K_ROPE, w_kr, half)
                    bank_read(pe, b, LATENT + half)
                    for form in range(2):
                        job = first + Q_ROPE + form
                        bank_free(job)
                        product(psum[:, bank_of[job], :], w_qr[:, 0, form], w_qr[:, 1, form],
                                latent_t[0:64, 0, cols], latent_t[0:64, 1, cols], True, True).then_inc(job_done, 1)
                    for n in range(4):
                        job = first + K_HEADS + n
                        p0, w = (64, w_kv[64:128, :, 0]) if n < 2 else (0, w_q[:])
                        m = slice(128 * (n % 2), 128 * (n % 2) + 128)
                        bank_free(job)
                        product(psum[:, bank_of[job], :], w[:, 0, m], w[:, 1, m],
                                latent_t[p0:p0 + 64, 0, cols], latent_t[p0:p0 + 64, 1, cols], True, True).then_inc(job_done, 1)
                for n in range(4):
                    bank_free(V_ROWS + n)
                    for i in range(2):
                        rows = slice(128 * (2 * n + i), 128 * (2 * n + i) + 128)
                        last = product(psum[:, bank_of[V_ROWS + n], 256 * i:256 * i + 256],
                                       latent_t[64:128, 0, rows], latent_t[64:128, 1, rows],
                                       w_kv[64:128, 0, 1], w_kv[64:128, 1, 1], True, True)
                    last.then_inc(job_done, 1)
                bank_read(pe, b, OUT_T - 1)
                STACK_DMAS = 4 * BLOCKS

                def scores(s):
                    c, g, j = steps[s]
                    q0 = 128 * max(0, j - 4 * c)
                    if s >= 1:
                        pe.wait_ge(exp_done, b * 2 * STEPS + 2 * s - 1)
                    for u in range(4):
                        h = 4 * g + u
                        bank = 2 * ((2 * s + u // 2) % 3) + u % 2
                        mm = pe.matmul(psum[:, bank, q0:512], k_stack[:, h, 128 * j:128 * j + 128],
                                       q_stack[:, h, 512 * c + q0:512 * c + 512], start=True, stop=True)
                        if u % 2:
                            mm.then_inc(scores_ready, 1)

                def weigh(s):
                    c, g, j = steps[s]
                    ci = c * GROUPS + g
                    q0 = 128 * max(0, j - 4 * c)
                    if j == 0 and ci >= 2:
                        pe.wait_ge(attn_ready, b * ACCS + ci - 1)
                    pe.wait_ge(clip_done, b * 2 * STEPS + 2 * s + 2)
                    for u in range(4):
                        mm = pe.matmul(psum[32 * u:32 * u + 32, 6 + ci % 2, q0:512], v[:, j, 4 * g + u, :],
                                       probs[:, (2 * s + u // 2) % PROB_SETS, u % 2, q0:512],
                                       start=(j == 0), stop=(j == 4 * c + 3))
                    mm.then_inc(pv_done, 1)

                def turn(ci):
                    pe.wait_ge(acc_copied, b * ACCS + ci + 1)
                    for t in range(4):
                        mm = pe.transpose(psum[:, 6 + ci % 2, 128 * t:128 * t + 128],
                                          acc_sb[:, ci % 2, 128 * t:128 * t + 128], ident[:])
                    mm.then_inc(acc_turned, 1)

                for s in range(STEPS):
                    if steps[s][1:] == (0, 0):
                        pe.wait_ge(stacked[steps[s][0]], (b + 1) * 16 * STACK_DMAS)
                    scores(s)
                    if s >= PV_LAG:
                        weigh(s - PV_LAG)
                    for ci in range(ACCS):
                        if s == last_step[ci] + PV_LAG + 2:
                            turn(ci)
                for s in range(STEPS - PV_LAG, STEPS):
                    weigh(s)
                for ci in range(ACCS):
                    if last_step[ci] + PV_LAG + 2 >= STEPS:
                        turn(ci)
                pe.wait_ge(attn_ready, b * ACCS + ACCS)
                for n in range(4):
                    half, k = divmod(n, 2)
                    for t in range(4):
                        last = pe.transpose(psum[:, bank_of[OUT_T + n], 128 * t:128 * t + 128],
                                            attn[:, 4 * half + t, 128 * k:128 * k + 128], ident[:])
                    last.then_inc(job_done, 1)
                for n in range(4):
                    for i in range(2):
                        rows = slice(128 * (2 * n + i), 128 * (2 * n + i) + 128)
                        for k in range(2):
                            if i == 0:
                                bank_read(pe, b, OUT_T + 2 * (n // 2) + k)
                            last = product(psum[:, bank_of[OUT_ROWS + n], 256 * i:256 * i + 256],
                                           attn_t[:, 0, k, rows], attn_t[:, 1, k, rows],
                                           w_o[:, 0, k], w_o[:, 1, k], k == 0, k == 1)
                    last.then_inc(job_done, 1)
def feed_forward(nc, x1_dram, consts_dram, w_dram, out_dram):
    blk_v = x1_dram.rearrange("(i t p) d -> i p t d", p=P, t=BT)
    out_v = out_dram.rearrange("(i t p) d -> i p t d", p=P, t=BT)
    PAIRS = TOKENS // (2 * BLOCK)
    G3 = 3 * D
    SLOTS = 3
    E_ROWS = 40
    S_ROWS = 97
    BEFORE, AFTER, NEXT = 0, 1, 2

    shared_first = (MC, 0, 1, 2, 3)
    units = [(it, q, t) for it in range(2) for q in range(2) for t in range(BT)]
    UNITS = len(units)
    order = [("x_t", q, 0, k) for q in range(2) for k in range(2)]
    for q in range(2):
        order += [("router", q)] + [("hidden", q, 0, m) for m in shared_first] + [("logits", q), ("halt", q, 0)]
    for q in range(2):
        order += [("mask_t", q)] + [("spread", q, s, m) for s in range(2) for m in range(MC)]
    order += [("unit", u) for u in range(7)] + [("x_t", 0, 1, k) for k in range(4)] + [("unit", 7)]
    order += [("hidden", 0, 1, m) for m in shared_first] + [("halt", 0, 1)]
    order += [("x_t", 1, 1, k) for k in range(4)] + [("hidden", 1, 1, m) for m in shared_first] + [("halt", 1, 1)]
    order += [("unit", u) for u in range(8, 15)] + [("x_t", 0, 2, k) for k in range(2)] + [("unit", 15)]
    order += [("hidden", 0, 2, m) for m in range(MC)] + [("refine", 0, n) for n in range(BT // 2)]
    order += [("x_t", 1, 2, k) for k in range(2)]
    order += [("hidden", 1, 2, m) for m in range(MC)] + [("refine", 1, n) for n in range(BT // 2)]
    jobs = [item for item in order if item[0] != "unit"]
    JOBS = len(jobs)
    number = {job: n for n, job in enumerate(jobs)}

    def frees(job):
        kind = job[0]
        if kind in ("x_t", "logits", "mask_t", "refine"):
            return "dve"
        if kind == "spread":
            return "act" if job[3] % 2 else "dve"
        return "act"

    act_reads = [j for j in jobs if j[0] == "x_t" or frees(j) == "act"]
    dve_reads = [j for j in jobs if frees(j) == "dve"]
    hidden = [j for j in jobs if j[0] == "hidden"]
    expert_rows = [j for j in hidden if j[3] != MC]
    gel_of, gel_before, turn = {}, {}, 0
    last_user = {}
    for n, job in enumerate(hidden):
        place = 2 if job[3] == MC else turn % 2
        turn += place != 2
        gel_of[job] = place
        gel_before[job] = last_user.get(place)
        last_user[place] = n

    with ExitStack() as ctx:
        def sb(name, shape, dt=F32):
            return ctx.enter_context(nc.sbuf_tensor(name, shape, dt))

        def sem(name):
            return ctx.enter_context(nc.semaphore(name))

        psum = ctx.enter_context(nc.psum_tensor("psum_f", [P, 8, 512], F32))
        B_BANK, AG_BANK = 3, 5
        soft_psum = psum[:, B_BANK:B_BANK + 2, :].rearrange("p a n -> p (a n)")
        ident = sb("ident_f", [P, P])
        w1 = sb("w1", [P, 2, 4, 5 * P], F32R)
        b1 = sb("b1", [P, MC + 1])
        w2 = sb("w2", [P, 2, MC, G3], F32R)
        ws2 = sb("ws2", [P, 2, G3], F32R)
        bias2 = sb("bias2", [P, G3], F32R)
        halt_w2 = sb("halt_w2", [P, 1])
        halt_b2 = sb("halt_b2", [P, 1])
        wr1 = sb("wr1", [P, 2, 2, HIDDEN], F32R)
        br1 = sb("br1", [HIDDEN, 1])
        wr2 = sb("wr2", [HIDDEN, EXPERTS])
        br2 = sb("br2", [P, EXPERTS])
        wf1 = sb("wf1", [P, 2, 2, 2 * D], F32R)
        bf1 = sb("bf1", [P, MC])
        wf2 = sb("wf2", [P, 2, MC, D], F32R)
        mu = sb("mu_all", [P, D])
        bf2 = sb("bf2", [P, D])
        share = sb("share", [P, 4])
        spread_w = sb("spread_w", [P, MC, P], BF16)
        expert_no = sb("expert_no", [P, EXPERTS])
        half_neg = sb("half_neg_f", [P, BT])
        one = sb("one_f", [P, 1])
        xs = [sb(f"xs{q}", [P, BT, D]) for q in range(2)]
        vs = [sb(f"vs{q}", [P, BT, D]) for q in range(2)]
        masks = [sb(f"masks{q}", [P, 2, MC, BLOCK], BF16) for q in range(2)]
        mask_t = [sb(f"mask_t{q}", [P, BLOCK], F32R) for q in range(2)]
        hid = [sb(f"hid{q}", [P, 2, MC, BLOCK], F32R) for q in range(2)]
        shid = [sb(f"shid{q}", [P, 2, BLOCK], F32R) for q in range(2)]
        alpha = [sb(f"alpha{q}", [P, BT, SLOTS]) for q in range(2)]
        coef = [sb(f"coef{q}", [P, 2, BT, SLOTS]) for q in range(2)]
        gap = [sb(f"gap{q}", [P, 2, BT]) for q in range(2)]
        haltv = [sb(f"haltv{q}", [P, 2, BT]) for q in range(2)]
        ctx_t = sb("ctx_t", [P, 2, 4, BLOCK], F32R)
        gel = sb("gel", [P, 3, BLOCK])
        picked = sb("picked", [P, 2, 2, MC, P], F32R)
        gates = sb("gates", [P, 2, SLOTS, 2 * D])
        soft = sb("soft", [P, SLOTS, D])
        relu = sb("relu", [P, 2, SLOTS, D])
        tmp = sb("tmp", [P, SLOTS, D])
        res = [gates[:, q].rearrange("p s n -> p (s n)")[:, 0:BT * D].rearrange("p (t n) -> p t n", n=D) for q in range(2)]
        x_in = [masks[0][:].rearrange("p s m n -> p (s m n)").bitcast(F32)[:, BT * D * q:BT * D * (q + 1)]
                .rearrange("p (t n) -> p t n", n=D) for q in range(2)]
        router_h = relu[0:HIDDEN, 0, 0:2].rearrange("p s n -> p (s n)")
        mask_b = soft[:].rearrange("p s n -> p (s n)").bitcast(BF16)[:, 0:BLOCK]
        xm = sb("xm", [P, D])
        vh = sb("vh", [P, D])
        stats = sb("stats_f", [P, BT, 6])
        moments = sb("moments_f", [P, 3, BT])
        mean = sb("mean_f", [P, 3, 2, BT])
        veps = sb("veps_f", [P, 3, 2, BT])
        rstd = sb("rstd_f", [P, 3, 2, BT])
        lg = sb("lg", [P, BT, EXPERTS])
        top = sb("top", [P, BT, 8])
        topi = sb("topi", [P, BT, 8], U32)
        topf = sb("topf", [P, BT, 8])
        onehot = tmp[:].rearrange("p s n -> p (s n)")[:, 0:BT * P].rearrange("p (t n) -> p t n", n=P)

        cleared = sem("f_cleared")
        weights_in = sem("f_weights_in")
        split_step = sem("f_split_step")
        weights_ready = sem("f_weights_ready")
        share_tanh = sem("f_share_tanh")
        pair_added = sem("f_pair_added")
        spread_free = sem("f_spread_free")
        x_loaded = sem("f_x_loaded")
        res_loaded = [sem(f"f_res_loaded{q}") for q in range(2)]
        stored = sem("f_stored")
        sp_step = sem("f_sp_step")
        stats_ready = sem("f_stats_ready")
        rstd_ready = sem("f_rstd_ready")
        xn_ready = sem("f_xn_ready")
        y_ready = [sem(f"f_y_ready{q}") for q in range(2)]
        job_done = sem("f_job_done")
        act_read = sem("f_act_read")
        dve_read = sem("f_dve_read")
        dve_step = sem("f_dve_step")
        act_step = sem("f_act_step")
        pe_step = sem("f_pe_step")
        pool_step = sem("f_pool_step")
        lower_made = sem("f_lower_made")
        shared_lower_made = sem("f_shared_lower_made")
        onehot_ready = sem("f_onehot_ready")
        gap_ready = sem("f_gap_ready")
        gap_tanh = sem("f_gap_tanh")
        upper_picked = sem("f_upper_picked")
        lower_picked = sem("f_lower_picked")
        slot_done = sem("f_slot_done")
        gate_read = sem("f_gate_read")
        b_read = sem("f_b_read")
        ln_done = sem("f_ln_done")
        softplus_ready = sem("f_softplus_ready")
        unit_done = sem("f_unit_done")

        def job_ready(eng, b, job):
            eng.wait_ge(job_done, b * JOBS + number[job] + 1)

        def act_took(eng, b, job):
            eng.wait_ge(act_read, (b + 1) * len(act_reads) + act_reads.index(job) + 1)

        def dve_took(eng, b, job):
            eng.wait_ge(dve_read, (b + 1) * len(dve_reads) + dve_reads.index(job) + 1)

        def bank_read(eng, b, job):
            (act_took if frees(job) == "act" else dve_took)(eng, b, job)

        def lower_ready(eng, b, job):
            if job[3] == MC:
                eng.wait_ge(shared_lower_made, b * 4 + 2 * job[2] + job[1] + 1)
            else:
                eng.wait_ge(lower_made, b * len(expert_rows) + expert_rows.index(job) + 1)

        def of_unit(b, u, parts, part):
            return (b * UNITS + u) * parts + part + 1

        def bank(job):
            return psum[:, number[job] % 3, :]

        def tile_of(t):
            return slice(P * t, P * t + P)

        spare = [masks[q][:].rearrange("p s m n -> p (s m n)").bitcast(F32) for q in range(2)]
        raw_w1 = [spare[k // 3][:, 5 * P * (k % 3):5 * P * (k % 3) + 5 * P] for k in range(4)]
        raw_f2 = spare[1][:, 640:1664].rearrange("p (m n) -> p m n", m=MC)
        raw_r1 = spare[1][:, 1664:1792].rearrange("p (k n) -> p k n", k=2)
        iw = spare[1][:, 1792:2048]
        raw_w2 = gates[:].rearrange("p a s n -> p (a s n)").rearrange("p (m n) -> p m n", m=MC)
        raw_s2 = relu[0:S_ROWS, 0].rearrange("p s n -> p (s n)")
        raw_s2u = tmp[:].rearrange("p s n -> p (s n)")
        raw_b2 = relu[:, 1].rearrange("p s n -> p (s n)")
        raw_f1 = vs[0][:].rearrange("p t n -> p (t n)").rearrange("p (k n) -> p k n", k=2)
        raw_spread = vs[1][:, 0:2].rearrange("p t n -> p (t n)")

        W = w_dram
        loads = [(ident[:], consts_dram["ident"]), (expert_no[:], consts_dram["expert_no"].partition_broadcast(P))]
        for k in range(4):
            loads.append((raw_w1[k][:, 0:MC * P].rearrange("p (e h) -> p e h", e=EXPERTS),
                          W["expert_w1"][:, P * k:P * k + P, :].rearrange("e p h -> p e h")))
            loads.append((raw_w1[k][:, 512:576], W["shared_w1"][P * k:P * k + P]))
            if k < 2:
                loads.append((raw_w1[k][:, 576:640], W["halt_w1"][P * k:P * k + P]))
        loads += [
            (b1[0:64, MC:MC + 1], W["shared_b1"].unsqueeze(1)),
            (b1[64:128, MC:MC + 1], W["halt_b1"].unsqueeze(1)),
            (raw_w2, W["expert_w2"].rearrange("(m f) h n -> (f h) m n", f=2)),
            (raw_s2[0:64], W["shared_w2"]),
            (raw_s2u[64:128], W["shared_w2"]),
            (raw_s2[64:65], W["shared_b2"].unsqueeze(0)),
            (raw_s2[96:97], W["shared_b2"].unsqueeze(0)),
            (halt_w2[64:128], W["halt_w2"]),
            (halt_b2[:], W["halt_b2"].partition_broadcast(P)),
            (raw_r1, W["router_w1"].rearrange("(k p) h -> p k h", p=P)),
            (br1[:], W["router_b1"].unsqueeze(1)),
            (wr2[:], W["router_w2"]),
            (br2[:], W["router_b2"].partition_broadcast(P)),
            (raw_f1, W["refine_w1"].rearrange("(k p) n -> p k n", p=P)),
            (raw_f2, W["refine_w2"].rearrange("(m p) n -> p m n", p=P)),
            (mu[:], W["mu"].partition_broadcast(P)),
            (bf2[:], W["refine_b2"].partition_broadcast(P)),
            (iw, W["integration_weight"].partition_broadcast(P)),
            (share[:, 0:1], W["shared_weight"].partition_broadcast(P)),
        ]
        for m in range(MC):
            loads += [(b1[:, m:m + 1], W["expert_b1"][2 * m:2 * m + 2].rearrange("f h -> (f h)").unsqueeze(1)),
                      (bf1[:, m:m + 1], W["refine_b1"][P * m:P * m + P].unsqueeze(1))]
        loads += [(raw_b2[r:r + EXPERTS], W["expert_b2"]) for r in (0, 32, 64, 96)]
        loads += [(raw_spread[r:r + EXPERTS], consts_dram["spread"]) for r in (0, 64)]

        block = ctx.enter_context(nc.Block())

        @block.sync
        def _(sp):
            sp.dma_start(x1_dram[TOKENS:TOKENS + 2 * BLOCK], x1_dram[0:2 * BLOCK]).then_inc(pair_added, 16)
            sp.wait_ge(cleared, 1)
            for dst, src in loads:
                sp.dma_start(dst, src).then_inc(weights_in, 16)
            sp.wait_ge(pair_added, 16)
            sp.wait_ge(spread_free, 1)
            for q in range(2):
                sp.dma_start(x_in[q], blk_v[q]).then_inc(x_loaded, 16)
            with sp.Fori(0, PAIRS) as b:
                sp.wait_ge(lower_picked, of_unit(b, 11, 2, 1))
                sp.sem_inc(sp_step, 1)
                sp.wait_ge(upper_picked, of_unit(b, 11, 2, 1))
                sp.sem_inc(sp_step, 1)
                for q in range(2):
                    sp.dma_start(x_in[q], blk_v[2 * b + 2 + q]).then_inc(x_loaded, 16)
                for q in range(2):
                    sp.wait_ge(unit_done, of_unit(b, UNITS - 2 + q, 1, 0))
                    sp.sem_inc(sp_step, 1)
                    sp.dma_start(res[q], blk_v[2 * b + q]).then_inc(res_loaded[q], 16)
                for q in range(2):
                    sp.wait_ge(y_ready[q], b + 1)
                    sp.sem_inc(sp_step, 1)
                    sp.dma_start(out_v[2 * b + q], res[q]).then_inc(stored, 16)

        @block.gpsimd
        def _(pool):
            for k in (2, 3):
                pool.memset(raw_w1[k][:, 576:640], 0.0)
            pool.memset(relu[:], 0.0)
            pool.memset(raw_spread, 0.0)
            pool.memset(tmp[:], 0.0)
            pool.memset(half_neg[:], -0.5)
            pool.memset(one[:], 1.0).then_inc(cleared, 1)

            def inverse_root(count, which, q):
                pool.wait_ge(stats_ready, count)
                pool.tensor_tensor(rstd[:, which, q], veps[:, which, q], half_neg[:], ALU.pow).then_inc(rstd_ready, 1)

            def lower_parts(b, job):
                _, q, it, m = job
                act_took(pool, b, job)
                pool.tensor_tensor(hid[q][:, 1, m], gel[:, gel_of[job]], hid[q][:, 0, m].bitcast(F32),
                                   ALU.subtract).then_inc(lower_made, 1)

            def pick_lower(b, u, s):
                it, q, t = units[u]
                if t == 0 and s == 0:
                    lower_ready(pool, b, ("hidden", q, it, MC - 1))
                    bank_read(pool, b, ("spread", q, 1, MC - 1))
                    bank_read(pool, b, ("spread", q, 1, MC - 2))
                if u > 0:
                    pool.wait_ge(slot_done, of_unit(b, u - 1, SLOTS, s + 1))
                pool.tensor_tensor(picked[:, s, 1], hid[q][:, 1, :, tile_of(t)].bitcast(F32),
                                   masks[q][:, s, :, tile_of(t)], ALU.mult).then_inc(lower_picked, 1)

            def softplus(b, u):
                pool.wait_ge(ln_done, of_unit(b, u, 1, 0))
                pool.tensor_tensor(relu[:, u % 2], relu[:, u % 2], soft[:], ALU.add).then_inc(softplus_ready, 1)

            def last_step(q):
                pool.wait_ge(rstd_ready, 6 + 4 * b)
                for src, op in ((mean, ALU.subtract), (rstd, ALU.mult)):
                    pool.tensor_tensor(vs[q][:], vs[q][:], src[:, AFTER, q].unsqueeze(2).to_broadcast([P, BT, D]),
                                       op).then_inc(pool_step, 1)
                    pool.wait_ge(pool_step, 2 * b + (1 if op == ALU.subtract else 2))
                pool.tensor_tensor(res[q], vs[q][:], res[q], ALU.add).then_inc(y_ready[q], 1)

            for q in range(2):
                inverse_root(q + 1, NEXT, q)
            with pool.Fori(0, PAIRS) as b:
                for it in range(2):
                    first = it * UNITS // 2
                    last = first + UNITS // 2 - 1
                    for q in range(2):
                        for m in range(MC):
                            lower_parts(b, ("hidden", q, it, m))
                        if q == it - 1:
                            for s in range(2):
                                pick_lower(b, first, s)
                    if it == 0:
                        for s in range(2):
                            pick_lower(b, first, s)
                    for u in range(first, last + 1):
                        if u < last:
                            for s in range(2):
                                pick_lower(b, u + 1, s)
                        if u == UNITS - 2:
                            for q in range(2):
                                inverse_root(4 * b + 3 + q, NEXT, q)
                        softplus(b, u)
                for q in range(2):
                    for m in range(MC):
                        lower_parts(b, ("hidden", q, 2, m))
                        if (q, m) == (1, 2):
                            inverse_root(4 * b + 5, AFTER, 0)
                inverse_root(4 * b + 6, AFTER, 1)
                last_step(1)
            pool.wait_ge(stored, 32 * PAIRS + 32)

        @block.scalar
        def _(act):
            act.wait_ge(weights_in, 16 * len(loads))
            act.activation(share[:, 1:2], share[:, 0:1], ACT.Tanh, scale=0.5).then_inc(share_tanh, 1)
            act.wait_ge(weights_ready, 1)
            act.sem_inc(act_read, len(act_reads))

            with act.Fori(0, PAIRS) as b:
                def x_upper(q, it, k):
                    job = ("x_t", q, it, k)
                    job_ready(act, b, job)
                    at = k if it == 1 else 2 * q + k
                    act.activation(ctx_t[:, 0, at], bank(job), ACT.Copy).then_inc(act_read, 1)

                def hidden_rows(q, it, m):
                    job = ("hidden", q, it, m)
                    if gel_before[job] is not None:
                        lower_ready(act, b, hidden[gel_before[job]])
                    job_ready(act, b, job)
                    bias = (b1 if it < 2 else bf1)[:, m:m + 1]
                    act.activation(gel[:, gel_of[job]], bank(job), ACT.Gelu, bias=bias)
                    if m == MC:
                        dst, src, bias = shid[q][0:64, 0], bank(job)[0:64], b1[0:64, m:m + 1]
                        act.activation(shid[q][0:64, 1], src, ACT.Gelu, bias=bias)
                    else:
                        dst, src = hid[q][:, 0, m], bank(job)
                    act.activation(dst, src, ACT.Gelu, bias=bias).then_inc(act_read, 1)

                def halt_tanh(q, it):
                    job = ("halt", q, it)
                    job_ready(act, b, job)
                    act.activation(haltv[q][:, 0], bank(job)[:, 0:BT], ACT.Tanh, bias=halt_b2[:],
                                   scale=0.5).then_inc(act_read, 1)

                def control(u):
                    it, q, t = units[u]
                    if u >= 2:
                        act.wait_ge(unit_done, of_unit(b, u - 2, 1, 0))
                    if u == 0:
                        act.wait_ge(stored, 32 * b + 32)
                    par = u % 2
                    first = D if it == 0 else 0
                    for s in range(SLOTS):
                        act.wait_ge(slot_done, of_unit(b, u, SLOTS, s))
                        act.activation(gates[:, par, s, first:2 * D], psum[:, AG_BANK + s, first:2 * D], ACT.Tanh,
                                       scale=0.5).then_inc(gate_read, 1)
                        if s == 1 and u > 0:
                            act.wait_ge(softplus_ready, of_unit(b, u - 1, 1, 0))
                        if s > 0:
                            n = slice(0, 2) if s == 1 else slice(2, 3)
                            src = soft_psum[:, n.start * D:n.stop * D]
                            act.activation(relu[:, par, n], src.rearrange("p (s n) -> p s n", n=D), ACT.Relu)
                            act.activation(soft[:, n], src.rearrange("p (s n) -> p s n", n=D),
                                           ACT.Abs).then_inc(b_read, 1)
                    act.wait_ge(b_read, of_unit(b, u, 2, 1))
                    act.activation(soft[:], soft[:], ACT.Exp, scale=-1.0).then_inc(act_step, 1)
                    act.wait_ge(act_step, of_unit(b, u, 1, 0))
                    act.activation(soft[:], soft[:], ACT.Ln, bias=one[:]).then_inc(ln_done, 1)

                for job in [item for item in order if item[0] == "unit" or item in act_reads]:
                    kind, q = job[0], job[1]
                    if kind == "unit":
                        control(job[1])
                    if job == ("spread", 0, 0, 1):
                        for p in range(2):
                            act.wait_ge(gap_ready, 2 * b + p + 1)
                            act.activation(gap[p][:, 1], gap[p][:, 0], ACT.Tanh, scale=0.5).then_inc(gap_tanh, 1)
                    if kind == "x_t":
                        x_upper(*job[1:])
                    if kind == "router":
                        if q == 1:
                            job_ready(act, b, ("logits", 0))
                        job_ready(act, b, job)
                        act.activation(router_h, bank(job)[0:HIDDEN], ACT.Gelu, bias=br1[:]).then_inc(act_read, 1)
                    if kind == "hidden":
                        hidden_rows(*job[1:])
                    if kind == "halt":
                        halt_tanh(*job[1:])
                    if kind == "spread":
                        job_ready(act, b, job)
                        act.activation(masks[q][:, job[2], job[3]], bank(job), ACT.Copy).then_inc(act_read, 1)

        @block.vector
        def _(dve):
            dve.wait_ge(weights_in, 16 * len(loads))
            split = [0]

            def after(ins):
                split[0] += 1
                ins.then_inc(split_step, 1)
                dve.wait_ge(split_step, split[0])

            for m in range(MC):
                dve.tensor_tensor(raw_f2[:, m], raw_f2[:, m], iw, ALU.mult)
            dve.tensor_tensor(bf2[:], bf2[:], iw, ALU.mult)
            dve.tensor_scalar(halt_b2[:], halt_b2[:], 0.5, None, ALU.mult)
            after(dve.tensor_copy(spread_w[:], raw_spread.rearrange("p (m n) -> p m n", m=MC)))
            shares = [(w1[:, :, k], raw_w1[k]) for k in range(4)]
            shares += ((w2, raw_w2), (ws2[0:S_ROWS], raw_s2), (wr1, raw_r1), (wf1, raw_f1), (wf2, raw_f2))
            for parts, raw in shares:
                dve.tensor_copy(parts[:, 0], raw)
            after(dve.tensor_copy(bias2[:], raw_b2))
            for parts, raw in shares:
                dve.tensor_tensor(parts[:, 1], raw, parts[:, 0].bitcast(F32), ALU.subtract)
            for r in (32, 96):
                last = dve.tensor_tensor(bias2[r:r + EXPERTS], raw_b2[r:r + EXPERTS], bias2[r:r + EXPERTS].bitcast(F32),
                                         ALU.subtract)
            after(last)
            after(dve.tensor_copy(ws2[64:65, 1], ws2[64:65, 0].bitcast(F32)))
            after(dve.tensor_copy(ws2[64:128, 0], raw_s2u[64:128]))
            after(dve.memset(tmp[:], 0.0))
            for q in range(2):
                zeros = tmp[64:128].rearrange("p s n -> p (s n)")[:, 0:BLOCK]
                dve.tensor_scalar(shid[q][64:128, 1], zeros, 1.0, None, ALU.add)
            dve.wait_ge(share_tanh, 1)
            dve.tensor_scalar(share[:, 2:3], share[:, 1:2], -0.25, 0.25, ALU.mult, ALU.add)
            dve.tensor_scalar(share[:, 3:4], share[:, 1:2], 0.25, -0.25, ALU.mult, ALU.add)
            for q in range(2):
                last = dve.tensor_scalar(alpha[q][:, :, 0], share[:, 1:2].to_broadcast([P, BT]), 0.5, 0.5, ALU.mult, ALU.add)
            after(last)
            dve.sem_inc(weights_ready, 2)
            dve.sem_inc(spread_free, 1)
            dve.sem_inc(dve_read, len(dve_reads))
            dve.sem_inc(stored, 32)

            def row_moments(src, which, q, then_wait):
                for t in range(BT):
                    last = dve.bn_stats(stats[:, t, :], src[:, t, :])
                then_wait(last)
                dve.tensor_tensor(moments[:, 0], stats[:, :, 1], stats[:, :, 4], ALU.add)
                dve.tensor_tensor(moments[:, 1], stats[:, :, 1], stats[:, :, 4], ALU.subtract)
                then_wait(dve.tensor_tensor(moments[:, 2], stats[:, :, 2], stats[:, :, 5], ALU.add))
                dve.tensor_scalar(mean[:, which, q], moments[:, 0], 0.5, None, ALU.mult)
                dve.tensor_scalar(moments[:, 2], moments[:, 2], 1.0 / D, EPS, ALU.mult, ALU.add)
                then_wait(dve.tensor_tensor(moments[:, 1], moments[:, 1], moments[:, 1], ALU.mult))
                dve.scalar_tensor_tensor(out=veps[:, which, q], in0=moments[:, 1], scalar=0.25, in1=moments[:, 2],
                                         op0=ALU.mult, op1=ALU.add).then_inc(stats_ready, 1)

            def normalize(dst, src, which, q):
                for t in range(BT):
                    last = dve.tensor_scalar(dst[:, t, :], src[:, t, :], mean[:, which, q, t:t + 1],
                                             rstd[:, which, q, t:t + 1], ALU.subtract, ALU.mult)
                return last

            def next_becomes_this():
                dve.tensor_copy(mean[:, BEFORE], mean[:, NEXT])
                return dve.tensor_copy(rstd[:, BEFORE], rstd[:, NEXT])

            dve.wait_ge(x_loaded, 32)
            for q in range(2):
                row_moments(x_in[q], NEXT, q, after)
            for q in range(2):
                dve.wait_ge(rstd_ready, q + 1)
                normalize(xs[q], x_in[q], NEXT, q).then_inc(xn_ready, 1)
            after(next_becomes_this())

            with dve.Fori(0, PAIRS) as b:
                made = [0]

                def then_wait(ins):
                    made[0] += 1
                    ins.then_inc(dve_step, 1)
                    dve.wait_ge(dve_step, b * DVE_STEPS_F + made[0])

                def x_lower(q, it, k):
                    job = ("x_t", q, it, k)
                    act_took(dve, b, job)
                    at = k if it == 1 else 2 * q + k
                    dve.tensor_tensor(ctx_t[:, 1, at], bank(job), ctx_t[:, 0, at].bitcast(F32), ALU.subtract).then_inc(dve_read, 1)

                def shared_lower(q, it):
                    act_took(dve, b, ("hidden", q, it, MC))
                    dve.tensor_tensor(shid[q][64:128, 0], gel[0:64, 2], shid[q][0:64, 0].bitcast(F32),
                                      ALU.subtract).then_inc(shared_lower_made, 1)

                def route(q):
                    job_ready(dve, b, ("logits", q))
                    dve.tensor_tensor(lg[:], bank(("logits", q))[:, 0:BT * EXPERTS].rearrange("p (t e) -> p t e", t=BT),
                                      br2[:].unsqueeze(1).to_broadcast([P, BT, EXPERTS]), ALU.add).then_inc(dve_read, 1)
                    dve_took(dve, b, ("logits", q))
                    dve.sem_inc(dve_step, 1)
                    made[0] += 1
                    for t in range(BT):
                        last = dve.max(top[:, t, :], lg[:, t, :])
                    then_wait(last)
                    dve.sem_inc(dve_step, 1)
                    made[0] += 1
                    for t in range(BT):
                        last = dve.max_index(topi[:, t, :], top[:, t, :], lg[:, t, :])
                    dve.tensor_tensor(gap[q][:, 0], top[:, :, 0], top[:, :, 1], ALU.subtract).then_inc(gap_ready, 1)
                    then_wait(last)
                    then_wait(dve.tensor_copy(topf[:], topi[:]))
                    if q == 1:
                        job_ready(dve, b, ("mask_t", 0))
                    for s in range(2):
                        dst = onehot[:, :, 64 * s:64 * s + 64].rearrange("p t (r e) -> p t r e", r=2)[:, :, :, 0:EXPERTS]
                        last = dve.tensor_tensor(
                            dst, topf[:, :, s:s + 1].unsqueeze(2).to_broadcast([P, BT, 2, EXPERTS]),
                            expert_no[:].unsqueeze(1).unsqueeze(1).to_broadcast([P, BT, 2, EXPERTS]), ALU.is_equal)
                    last.then_inc(onehot_ready, 1)

                def coefficients(q, it):
                    act_took(dve, b, ("halt", q, it))
                    then_wait(dve.tensor_scalar(haltv[q][:, 1], haltv[q][:, 0], 0.5, 0.5, ALU.mult, ALU.add))
                    then_wait(dve.tensor_tensor(coef[q][:, 0], alpha[q][:], haltv[q][:, 1].unsqueeze(2).to_broadcast([P, BT, SLOTS]),
                                                ALU.mult))
                    then_wait(dve.tensor_scalar(coef[q][:, 1], coef[q][:, 0], HALF_STEP, None, ALU.mult))

                def pick_upper(u, s):
                    it, q, t = units[u]
                    if t == 0 and s == 0:
                        act_took(dve, b, ("hidden", q, it, MC - 1))
                        bank_read(dve, b, ("spread", q, 1, MC - 1))
                        bank_read(dve, b, ("spread", q, 1, MC - 2))
                    if u > 0:
                        dve.wait_ge(slot_done, of_unit(b, u - 1, SLOTS, s + 1))
                    dve.tensor_tensor(picked[:, s, 0], hid[q][:, 0, :, tile_of(t)].bitcast(F32),
                                      masks[q][:, s, :, tile_of(t)], ALU.mult).then_inc(upper_picked, 1)

                def integrate(u):
                    it, q, t = units[u]
                    par = u % 2
                    x, v = xs[q][:, t, :], vs[q][:, t, :]
                    sp_b, ta, tg = relu[:, par], gates[:, par, :, 0:D], gates[:, par, :, D:2 * D]
                    c = [coef[q][:, 0, t, s:s + 1] for s in range(SLOTS)]
                    d = [coef[q][:, 1, t, s:s + 1] for s in range(SLOTS)]
                    if u > 0:
                        dve.wait_ge(unit_done, of_unit(b, u - 1, 1, 0))
                    dve.tensor_tensor(xm[:], x, mu[:], ALU.subtract)
                    if it == 1:
                        then_wait(dve.tensor_scalar(vh[:], v, 0.5, None, ALU.mult))
                    dve.wait_ge(softplus_ready, of_unit(b, u, 1, 0))
                    dve.wait_ge(gate_read, of_unit(b, u, SLOTS, SLOTS - 1))
                    if it == 0:
                        then_wait(dve.scalar_tensor_tensor(out=tmp[:], in0=tg, scalar=1.0, in1=sp_b, op0=ALU.add, op1=ALU.mult))
                        dve.tensor_scalar(sp_b[:, 0], sp_b[:, 0], c[0], None, ALU.mult)
                        then_wait(dve.tensor_scalar(tmp[:, 0], tmp[:, 0], d[0], None, ALU.mult))
                        for s in (1, 2):
                            dve.scalar_tensor_tensor(out=sp_b[:, 0], in0=sp_b[:, s], scalar=c[s], in1=sp_b[:, 0],
                                                     op0=ALU.mult, op1=ALU.add)
                            then_wait(dve.scalar_tensor_tensor(out=tmp[:, 0], in0=tmp[:, s], scalar=d[s], in1=tmp[:, 0],
                                                               op0=ALU.mult, op1=ALU.add))
                        dve.scalar_tensor_tensor(out=v, in0=sp_b[:, 0], scalar=-1.0, in1=xm[:], op0=ALU.mult, op1=ALU.mult)
                        then_wait(dve.tensor_tensor(tmp[:, 1], tmp[:, 0], xm[:], ALU.mult))
                        dve.tensor_tensor(x, x, tmp[:, 1], ALU.subtract).then_inc(unit_done, 1)
                    else:
                        def wide(a):
                            return a[:].unsqueeze(1).to_broadcast([P, SLOTS, D])
                        dve.tensor_tensor(sp_b, sp_b, wide(xm), ALU.mult)
                        then_wait(dve.scalar_tensor_tensor(out=tmp[:], in0=ta, scalar=1.0, in1=wide(vh), op0=ALU.add, op1=ALU.mult))
                        then_wait(dve.tensor_tensor(tmp[:], tmp[:], sp_b, ALU.subtract))
                        then_wait(dve.scalar_tensor_tensor(out=tmp[:], in0=tg, scalar=1.0, in1=tmp[:], op0=ALU.add, op1=ALU.mult))
                        for s in range(SLOTS):
                            last = dve.scalar_tensor_tensor(out=x, in0=tmp[:, s], scalar=d[s], in1=x, op0=ALU.mult, op1=ALU.add)
                            if s < SLOTS - 1:
                                then_wait(last)
                        last.then_inc(unit_done, 1)

                def layernorm_again(q):
                    dve.wait_ge(res_loaded[q], 16 * b + 16)
                    then_wait(normalize(vs[q], res[q], BEFORE, q))
                    then_wait(dve.tensor_tensor(vs[q][:], vs[q][:], bf2[:].unsqueeze(1).to_broadcast([P, BT, D]), ALU.add))

                def add_refined(q):
                    for n in range(BT // 2):
                        job = ("refine", q, n)
                        job_ready(dve, b, job)
                        dve.tensor_tensor(vs[q][:, 2 * n:2 * n + 2, :], bank(job).rearrange("p (t n) -> p t n", n=D),
                                          vs[q][:, 2 * n:2 * n + 2, :], ALU.add).then_inc(dve_read, 1)

                for q in range(2):
                    for k in range(2):
                        x_lower(q, 0, k)
                then_wait(dve.memset(onehot, 0.0))
                for q in range(2):
                    shared_lower(q, 0)
                    route(q)
                for q in range(2):
                    job_ready(dve, b, ("mask_t", q))
                    dve.tensor_copy(mask_t[q][:], bank(("mask_t", q)))
                    if q == 1:
                        job_ready(dve, b, ("spread", 0, 1, MC - 1))
                    dve.tensor_copy(mask_b, bank(("mask_t", q))).then_inc(dve_read, 1)
                    for s in range(2):
                        for m in range(0, MC, 2):
                            job_ready(dve, b, ("spread", q, s, m))
                            dve.tensor_copy(masks[q][:, s, m], bank(("spread", q, s, m))).then_inc(dve_read, 1)
                for q in range(2):
                    dve.wait_ge(gap_tanh, 2 * b + q + 1)
                    dve.tensor_scalar(alpha[q][:, :, 1], gap[q][:, 1], share[:, 2:3], share[:, 2:3], ALU.mult, ALU.add)
                    then_wait(dve.tensor_scalar(alpha[q][:, :, 2], gap[q][:, 1], share[:, 3:4], share[:, 2:3], ALU.mult, ALU.add))
                    coefficients(q, 0)
                for it in range(2):
                    first = it * UNITS // 2
                    last_unit = first + UNITS // 2 - 1
                    if it == 1:
                        shared_lower(0, 1)
                    for s in range(2):
                        pick_upper(first, s)
                    if it == 1:
                        coefficients(0, 1)
                        for k in range(4):
                            x_lower(1, 1, k)
                        shared_lower(1, 1)
                        coefficients(1, 1)
                    for u in range(first, last_unit + 1):
                        if u < last_unit:
                            for s in range(2):
                                pick_upper(u + 1, s)
                        if u > first:
                            integrate(u - 1)
                        if u == 6:
                            for k in range(4):
                                x_lower(0, 1, k)
                        if u == 13:
                            dve.wait_ge(x_loaded, 32 * b + 64)
                            for q in range(2):
                                row_moments(x_in[q], NEXT, q, then_wait)
                        if u == 14:
                            for k in range(2):
                                x_lower(0, 2, k)
                    if it == 1:
                        dve.wait_ge(rstd_ready, 4 * b + 4)
                        normalize(xs[0], x_in[0], NEXT, 0).then_inc(xn_ready, 1)
                    integrate(last_unit)
                for q in range(2):
                    layernorm_again(q)
                add_refined(0)
                for k in range(2):
                    x_lower(1, 2, k)
                normalize(xs[1], x_in[1], NEXT, 1).then_inc(xn_ready, 1)
                dve_took(dve, b, ("refine", 0, BT // 2 - 1))
                row_moments(vs[0], AFTER, 0, then_wait)
                dve.wait_ge(rstd_ready, 4 * b + 5)
                then_wait(normalize(vs[0], vs[0], AFTER, 0))
                dve.tensor_tensor(res[0], vs[0][:], res[0], ALU.add).then_inc(y_ready[0], 1)
                add_refined(1)
                dve_took(dve, b, ("refine", 1, BT // 2 - 1))
                row_moments(vs[1], AFTER, 1, then_wait)
                then_wait(next_becomes_this())
                assert made[0] == DVE_STEPS_F, made[0]

        @block.tensor
        def _(pe):
            pe.wait_ge(weights_ready, 1)

            with pe.Fori(0, PAIRS) as b:
                def bank_free(job):
                    n = number[job]
                    if n >= 3:
                        bank_read(pe, b, jobs[n - 3])
                    else:
                        bank_read(pe, b - 1, jobs[max(m for m in range(JOBS) if m % 3 == n)])

                def turn_x(q, it, k):
                    src = xs[q] if k < 2 else vs[q]
                    job = ("x_t", q, it, k)
                    if k == 0:
                        if it == 0:
                            pe.wait_ge(xn_ready, 2 * b + q + 1)
                        else:
                            pe.wait_ge(unit_done, of_unit(b, 8 * (it - 1) + 4 * q + BT - 1, 1, 0))
                    bank_free(job)
                    for t in range(BT):
                        last = pe.transpose(bank(job)[:, tile_of(t)], src[:, t, P * (k % 2):P * (k % 2) + P], ident[:])
                    last.then_inc(job_done, 1)

                def from_x(job, w, m, width):
                    _, q, it = (*job, 0)[:3]
                    chunks = range(4) if it == 1 and job[0] == "hidden" else range(2)
                    first = 0 if it == 1 else 2 * q
                    for k in chunks:
                        dve_took(pe, b, ("x_t", q, it, k))
                        if k == 0:
                            bank_free(job)
                        x_hi, x_lo = ctx_t[:, 0, first + k], ctx_t[:, 1, first + k]
                        out = bank(job)[0:width]
                        pe.matmul(out, w[:, 0, k, m], x_hi, start=(k == 0), stop=False)
                        pe.matmul(out, w[:, 0, k, m], x_lo, start=False, stop=False)
                        last = pe.matmul(out, w[:, 1, k, m], x_hi, start=False, stop=(k == chunks[-1]))
                    last.then_inc(job_done, 1)

                def logits(q):
                    job = ("logits", q)
                    act_took(pe, b, ("router", q))
                    bank_free(job)
                    for t in range(BT):
                        last = pe.matmul(bank(job)[:, EXPERTS * t:EXPERTS * t + EXPERTS], router_h[:, tile_of(t)], wr2[:],
                                         start=True, stop=True)
                    last.then_inc(job_done, 1)

                def halt(q, it):
                    job = ("halt", q, it)
                    act_took(pe, b, ("hidden", q, it, MC))
                    bank_free(job)
                    pe.sem_inc(pe_step, 1)
                    for t in range(BT):
                        last = pe.matmul(bank(job)[:, t:t + 1], gel[64:128, 2, tile_of(t)], halt_w2[64:128], start=True, stop=True)
                    last.then_inc(job_done, 1)

                def mask_rows(q):
                    job = ("mask_t", q)
                    pe.wait_ge(onehot_ready, 2 * b + q + 1)
                    bank_free(job)
                    for t in range(BT):
                        last = pe.transpose(bank(job)[:, tile_of(t)], onehot[:, t, :], ident[:])
                    last.then_inc(job_done, 1)

                def spread(q, s, m):
                    job = ("spread", q, s, m)
                    dve_took(pe, b, ("mask_t", q))
                    bank_free(job)
                    pe.sem_inc(pe_step, 1)
                    pe.matmul(bank(job), spread_w[64 * s:64 * s + EXPERTS, m, :], mask_b[64 * s:64 * s + EXPERTS, :],
                              start=True, stop=True).then_inc(job_done, 1)

                def refine(q, n):
                    job = ("refine", q, n)
                    lower_ready(pe, b, ("hidden", q, 2, MC - 1))
                    bank_free(job)
                    for i in range(2):
                        out = bank(job)[:, D * i:D * i + D]
                        tok = tile_of(2 * n + i)
                        for m in range(MC):
                            pe.matmul(out, hid[q][:, 0, m, tok], wf2[:, 0, m], start=(m == 0), stop=False)
                            pe.matmul(out, hid[q][:, 0, m, tok], wf2[:, 1, m], start=False, stop=False)
                            last = pe.matmul(out, hid[q][:, 1, m, tok], wf2[:, 0, m], start=False, stop=(m == MC - 1))
                    last.then_inc(job_done, 1)

                def second_layer(u):
                    it, q, t = units[u]
                    tok = tile_of(t)
                    for s in range(SLOTS):
                        soft_out = soft_psum[:, D * s:D * s + D]
                        if it == 0:
                            gate_out = psum[:, AG_BANK + s, D:2 * D]
                        else:
                            gate_out = psum[:, AG_BANK + s, :].rearrange("p (c n) -> p c n", n=D)

                        def both(x, w, start=False, stop=False):
                            cols = w.rearrange("p (c n) -> p c n", n=D)
                            pe.matmul(soft_out, x, cols[:, 1], start=start, stop=stop)
                            return pe.matmul(gate_out, x, cols[:, 2] if it == 0 else cols[:, 0::2], start=start, stop=stop)

                        if u > 0:
                            pe.wait_ge(gate_read, of_unit(b, u - 1, SLOTS, s))
                            if s != 1:
                                pe.wait_ge(b_read, of_unit(b, u - 1, 2, s // 2))
                        if s == 0:
                            if t == 0:
                                lower_ready(pe, b, ("hidden", q, it, MC))
                            both(shid[q][:, 0, tok], ws2[:, 0], start=True)
                            last = both(shid[q][0:S_ROWS, 1, tok], ws2[0:S_ROWS, 1], stop=True)
                        else:
                            i = s - 1
                            pe.wait_ge(upper_picked, of_unit(b, u, 2, i))
                            for m in range(MC):
                                both(picked[:, i, 0, m], w2[:, 0, m], start=(m == 0))
                                both(picked[:, i, 0, m], w2[:, 1, m])
                            pe.wait_ge(lower_picked, of_unit(b, u, 2, i))
                            for m in range(MC):
                                both(picked[:, i, 1, m], w2[:, 0, m])
                            rows = slice(64 * i, 64 * i + E_ROWS)
                            last = both(mask_t[q][rows, tok], bias2[rows], stop=True)
                        last.then_inc(slot_done, 1)

                for job in order:
                    kind, rest = job[0], job[1:]
                    if kind == "unit":
                        second_layer(*rest)
                    if kind == "x_t":
                        turn_x(*rest)
                    if kind == "router":
                        from_x(job, wr1, slice(0, HIDDEN), HIDDEN)
                    if kind == "hidden":
                        m = rest[2]
                        from_x(job, w1 if rest[1] < 2 else wf1, slice(P * m, P * m + P), P)
                    if kind == "logits":
                        logits(*rest)
                    if kind == "halt":
                        halt(*rest)
                    if kind == "mask_t":
                        mask_rows(*rest)
                    if kind == "spread":
                        spread(*rest)
                    if kind == "refine":
                        refine(*rest)


def rope_tables():
    inv = np.float32(10000.0) ** (-np.arange(0, ROPE_DIM, 2, dtype=np.float32) / np.float32(ROPE_DIM))
    ang = np.arange(SEQ, dtype=np.float32)[None, :] * inv[:, None]
    cos = np.repeat(np.cos(ang), 2, axis=0)
    sin = np.repeat(np.sin(ang), 2, axis=0)
    sin[0::2] = -sin[0::2]
    up = np.float32(QK_UP)
    return np.tile(cos, (HEADS, 1)).astype(np.float32) * up, np.tile(sin, (HEADS, 1)).astype(np.float32) * up


def kernel(**inputs):
    import concourse.bacc as bacc
    from concourse.bass_utils import run_bass_kernel_spmd as run
    nc = bacc.Bacc("TRN2", target_bir_lowering=False, num_devices=1)
    arrays = {}

    def given(name, a):
        arrays[name + "_dram"] = np.ascontiguousarray(a)
        return nc.dram_tensor(name + "_dram", arrays[name + "_dram"].shape, F32, kind="ExternalInput").ap()

    cos, sin = rope_tables()
    spread = np.zeros((EXPERTS, MC * P), np.float32)
    for e in range(EXPERTS):
        spread[e, HIDDEN * e:HIDDEN * e + HIDDEN] = 1.0
    consts = {"ident": given("ident", np.eye(P, dtype=np.float32)), "cos": given("cos", cos), "sin": given("sin", sin),
              "spread": given("spread", spread), "expert_no": given("expert_no", np.arange(EXPERTS, dtype=np.float32))}
    x = given("x", np.asarray(inputs["L0_attn_x"]).reshape(TOKENS, D))
    attn_w, ffn_w = {}, {}
    for name, a in inputs.items():
        a = np.asarray(a)
        a = a.reshape(a.shape or (1,))
        if name.startswith("L0_ffn_"):
            ffn_w[name[len("L0_ffn_"):]] = given(name, a)
        elif name != "L0_attn_x":
            attn_w[name[len("L0_attn_"):]] = given(name, a)
    x1 = nc.dram_tensor("x1_scratch", (TOKENS + 2 * BLOCK, D), F32, kind="Internal").ap()
    out = nc.dram_tensor("out", (TOKENS, D), F32, kind="ExternalOutput").ap()
    attention(nc, x, consts, attn_w, x1[0:TOKENS])
    feed_forward(nc, x1, consts, ffn_w, out)
    r = run(nc, [arrays], core_ids=[0])
    return r.results[0]["out"].reshape(BATCH, SEQ, D)
```
